# Optimizing a Trainium2 kernel written in Bass

```python
import numpy as np
import jax
import jax.numpy as jnp

def _softmax(x, axis=-1):
    return jax.nn.softmax(x, axis=axis)

def _gelu(x):
    return jax.nn.gelu(x, approximate=True)

def _silu(x):
    return jax.nn.silu(x)

def _sigmoid(x):
    return jax.nn.sigmoid(x)

def _layernorm(x, axis=-1, eps=1e-05):
    m = jnp.mean(x, axis=axis, keepdims=True)
    v = jnp.var(x, axis=axis, keepdims=True)
    return (x - m) / jnp.sqrt(v + eps)

def _scatter_add(tgt, idx, src, axis=0):
    return tgt.at[idx].add(src)

def _segment_sum(src, seg, n):
    return jax.ops.segment_sum(src, seg, n)
kernel_name = 'mk_gnn_preln_d2_gnn_r32_1da0a9'

def setup_inputs(seed: int=0):
    np.random.seed(seed)
    _w = jnp.asarray

    def _rec_inputs():
        import jax
        import jax.numpy as jnp
        _gk = jax.random.key(seed)
        x = -0.000202 + 1 * jax.random.normal(jax.random.fold_in(_gk, 1), (50000, 64), jnp.float32)
        src = jax.random.randint(jax.random.fold_in(_gk, 2), (50000,), 0, 50000, jnp.int32)
        dst = jnp.minimum((50000 * jax.random.uniform(jax.random.fold_in(_gk, 3), (50000,)) ** 2.0).astype(jnp.int32), 49999)
        _o = jnp.argsort(dst, stable=True)
        src = src[_o]
        dst = dst[_o]
        return (x, src, dst)
    x, src, dst = _rec_inputs()

    def _L0_gnn_setup():
        import jax, jax.numpy as jnp
        import numpy as np
        N_NODES = 3125
        N_EDGES = 1250000
        D_IN = 64
        D_OUT = 64
        key = jax.random.key(seed)
        k1, k2, k3, k4, k5 = jax.random.split(key, 5)
        x = jax.random.normal(k1, (N_NODES, D_IN), dtype=jnp.float32)
        edge_index = jax.random.randint(k2, (2, N_EDGES), 0, N_NODES, dtype=jnp.int64)
        w_neigh = jax.random.normal(k3, (D_OUT, D_IN), dtype=jnp.float32) / np.sqrt(D_IN)
        w_self = jax.random.normal(k4, (D_OUT, D_IN), dtype=jnp.float32) / np.sqrt(D_IN)
        b_self = jax.random.normal(k5, (D_OUT,), dtype=jnp.float32) * 0.01
        return {'x': x, 'edge_index': edge_index, 'w_neigh': w_neigh, 'w_self': w_self, 'b_self': b_self}
    _L0_gnn_all = _L0_gnn_setup()
    _L0_gnn_in = {k: v for k, v in _L0_gnn_all.items() if k in ('w_neigh', 'w_self', 'b_self')}
    del _L0_gnn_all

    def _L1_gnn_setup():
        import jax, jax.numpy as jnp
        import numpy as np
        N, E, D = (50000, 25000, 64)
        key = jax.random.key(seed)
        ks = jax.random.split(key, 8)
        s = 1.0 / np.sqrt(2 * D)
        inp = {'node_emb': jax.random.normal(ks[0], (N, D), dtype=jnp.float32), 'edge_index': jax.random.randint(ks[1], (2, E), 0, N, dtype=jnp.int64), 'W1': jax.random.normal(ks[2], (2 * D, D), dtype=jnp.float32) * s, 'b1': jnp.zeros((D,), dtype=jnp.float32), 'W2': jax.random.normal(ks[3], (D, D), dtype=jnp.float32) * (1.0 / np.sqrt(D)), 'b2': jnp.zeros((D,), dtype=jnp.float32), 'Wg': jax.random.normal(ks[4], (D, D), dtype=jnp.float32) * (1.0 / np.sqrt(D)), 'bg': jnp.zeros((D,), dtype=jnp.float32)}
        return inp
    _L1_gnn_all = _L1_gnn_setup()
    _L1_gnn_in = {k: v for k, v in _L1_gnn_all.items() if k in ('W1', 'b1', 'W2', 'b2', 'Wg', 'bg')}
    del _L1_gnn_all
    return {'x': x, 'src': src, 'dst': dst, 'L0_gnn_w_neigh': _L0_gnn_in['w_neigh'], 'L0_gnn_w_self': _L0_gnn_in['w_self'], 'L0_gnn_b_self': _L0_gnn_in['b_self'], 'L1_gnn_W1': _L1_gnn_in['W1'], 'L1_gnn_b1': _L1_gnn_in['b1'], 'L1_gnn_W2': _L1_gnn_in['W2'], 'L1_gnn_b2': _L1_gnn_in['b2'], 'L1_gnn_Wg': _L1_gnn_in['Wg'], 'L1_gnn_bg': _L1_gnn_in['bg']}

def reference(x, src, dst, L0_gnn_w_neigh, L0_gnn_w_self, L0_gnn_b_self, L1_gnn_W1, L1_gnn_b1, L1_gnn_W2, L1_gnn_b2, L1_gnn_Wg, L1_gnn_bg):
    import jax
    import jax.numpy as jnp

    def _L0_gnn_ref(x, edge_index, w_neigh, w_self, b_self):
        import jax, jax.numpy as jnp
        import numpy as np
        N_NODES = 3125
        N_EDGES = 1250000
        D_IN = 64
        D_OUT = 64
        num_nodes = x.shape[0]
        src, dst = (edge_index[0], edge_index[1])
        agg = jax.ops.segment_sum(x[src], dst, num_segments=num_nodes)
        degree = jax.ops.segment_sum(jnp.ones_like(dst, dtype=x.dtype), dst, num_segments=num_nodes)
        degree = jnp.maximum(degree, 1.0)
        agg = agg / degree[:, None]
        return agg @ w_neigh.T + x @ w_self.T + b_self

    def _L1_gnn_ref(node_emb, edge_index, W1, b1, W2, b2, Wg, bg):
        import jax, jax.numpy as jnp
        import numpy as np
        src, dst = (edge_index[0], edge_index[1])
        pair_emb = jnp.concatenate([node_emb[src], node_emb[dst]], axis=-1)
        h = jax.nn.relu(pair_emb @ W1 + b1)
        interaction = h @ W2 + b2
        gate = jax.nn.sigmoid(interaction @ Wg + bg)
        gated = interaction * gate
        N = node_emb.shape[0]
        summed = jax.ops.segment_sum(gated, src, num_segments=N)
        counts = jax.ops.segment_sum(jnp.ones((src.shape[0],), dtype=gated.dtype), src, num_segments=N)
        pooled = summed / jnp.maximum(counts, 1.0)[:, None]
        return pooled
    edge_index = jnp.stack([src, dst])
    h = jnp.maximum(_layernorm(x, axis=-1), 0.0)
    x = x + _L0_gnn_ref(h, edge_index, L0_gnn_w_neigh, L0_gnn_w_self, L0_gnn_b_self)
    h = jnp.maximum(_layernorm(x, axis=-1), 0.0)
    x = x + _L1_gnn_ref(h, edge_index, L1_gnn_W1, L1_gnn_b1, L1_gnn_W2, L1_gnn_b2, L1_gnn_Wg, L1_gnn_bg)
    return x

_drawn_inputs = setup_inputs


def setup_inputs(seed=0):
    import zlib

    import numpy as np

    out = dict(_drawn_inputs(seed))
    spreads = {'L1_gnn_b1': (0.0, 0.433), 'L1_gnn_b2': (0.0, 0.1), 'L1_gnn_bg': (0.0, 0.8)}
    factors = {'L0_gnn_b_self': 7.755}
    for name, (base, spread) in spreads.items():
        noise = np.random.default_rng([zlib.crc32(name.encode()), seed]).standard_normal(out[name].shape)
        drawn = base * np.exp(spread * noise) if base else spread * noise
        out[name] = jnp.asarray(drawn.astype(out[name].dtype))
    for name, factor in factors.items():
        out[name] = (out[name] * factor).astype(out[name].dtype)
    return out
```

```python
from collections import namedtuple
from contextlib import ExitStack

import numpy as np

import concourse.bass as bass
from concourse import mybir

F32 = mybir.dt.float32
I32 = mybir.dt.int32
ALU = mybir.AluOpType
ACT = mybir.ActivationFunctionType
AX = mybir.AxisListType

N = 50000
D = 64
P = 128
COLS = N // P
TAIL = N - P * COLS
BT = 5
PAIRS = COLS // (2 * BT)
BATCHES = 2 * PAIRS + 1
ROW = D + 1
PEELED = 2
ZERO_ROWS = 392
ZERO_DMAS = 14
LATE_ROWS = 396
LATE_DMAS = PAIRS - 1 - PEELED
CHUNK = 39
CHUNKS = COLS // CHUNK
EPS = 1e-5

Batch = namedtuple("Batch", "layer pair u g parts tiles")


def batch(layer, pair, u):
    return Batch(layer, pair, u, layer * BATCHES + 2 * pair + u, P, BT)


def tail(layer):
    return Batch(layer, PAIRS, 0, layer * BATCHES + 2 * PAIRS, TAIL, 1)


def before(b, back=1):
    if isinstance(b.pair, int) and 2 * b.pair + b.u < back:
        return None
    at = b.u - back
    return batch(b.layer, b.pair + at // 2, at % 2)


def after_next(b):
    if isinstance(b.pair, int) and b.pair >= PAIRS - 1:
        return tail(b.layer) if (b.pair, b.u) == (PAIRS - 1, 0) else None
    return batch(b.layer, b.pair + 1, b.u)


def slot_free(b):
    return b.g if b.layer and isinstance(b.pair, int) and b.pair == 0 and b.u == 0 else b.g - 1


def gathered_by(b):
    earlier = (PAIRS * BT + (b.u == 0)) * b.layer
    return 16 * (earlier + (1 + b.layer) * (b.pair * BT + b.tiles))


def scatters(pair, tiles, table):
    return pair * BT + (tiles + 1 - table) // 2


def until(engine, semaphore, value):
    if isinstance(value, int) and value <= 0:
        return
    engine.wait_ge(semaphore, value)


def every_batch(engine, layer, step):
    for pair in range(PEELED):
        for u in range(2):
            step(batch(layer, pair, u))
    with engine.Fori(PEELED, PAIRS - 1) as pair:
        for u in range(2):
            step(batch(layer, pair, u))
    for u in range(2):
        step(batch(layer, PAIRS - 1, u))
    step(tail(layer))


def every_chunk(engine, step):
    for s in range(2):
        step(0, s)
    with engine.Fori(1, CHUNKS // 2) as pair:
        for s in range(2):
            step(pair, s)


def build(nc, x, src, dst, w_neigh, w_self, b_self, W1, b1, W2, b2, Wg, bg, out):
    ctx = ExitStack()
    with ctx:
        def sb(name, shape, dt=F32):
            return ctx.enter_context(nc.sbuf_tensor(name, shape, dt))

        def sem(name):
            return ctx.enter_context(nc.semaphore(name))

        def dram(name, shape):
            return nc.dram_tensor(name, shape, F32, kind="Internal").ap()

        tables = [[dram("sums_in_a", [ZERO_ROWS * P, ROW]), dram("sums_in_b", [ZERO_ROWS * P, ROW])],
                  [dram("sums_out_a", [LATE_ROWS * P, ROW]), dram("sums_out_b", [LATE_ROWS * P, ROW])]]
        x1 = dram("x1", [N, D])

        xs = sb("xs", [P, COLS, D])
        xs_tail = sb("xs_tail", [TAIL, D])
        edges = sb("edges", [P, 2, COLS], I32)
        edges_tail = sb("edges_tail", [TAIL, 2, 1], I32)
        take = sb("take", [P, 2, 2, BT], I32)
        rows = sb("rows", [P, 2, BT, 2, D])
        xc = sb("xc", [P, 2, BT, 2, D])
        sq = sb("sq", [P, BT, 2, D])
        row_sum = sb("row_sum", [P, 2 * BT])
        neg_mean = sb("neg_mean", [P, 2 * BT])
        sq_sum = sb("sq_sum", [P, 2 * BT])
        var = sb("var", [P, 2 * BT])
        half_bits = sb("half_bits", [P, 2 * BT], I32)
        guess = sb("guess", [P, 4, 2 * BT])
        y2 = sb("y2", [P, 2 * BT])
        vy2 = sb("vy2", [P, 2 * BT])
        hT = sb("hT", [P, BT * P])
        aT = sb("aT", [D + 1, BT * P])
        gate = sb("gate", [P, BT, D])
        msg = sb("msg", [P, BT, ROW])
        key = sb("key", [P, 2, BT])
        later = sb("later", [P, 2, BT, P])
        rank = sb("rank", [P, 2, BT])
        to_spare = sb("to_spare", [P, BT])
        shift = sb("shift", [P, BT])
        put = sb("put", [P, 2, BT], I32)
        summed = sb("summed", [P, 2, BT, ROW])
        chunk_a = sb("chunk_a", [P, 2, CHUNK, ROW])
        chunk_b = sb("chunk_b", [P, 2, CHUNK, ROW])
        count = sb("count", [P, CHUNK])
        count1 = sb("count1", [P, CHUNK])
        per_count = sb("per_count", [P, CHUNK])
        zeros = sb("zeros", [P, ZERO_ROWS * ROW // ZERO_DMAS])
        ident = sb("ident", [P, P])
        lower = sb("lower", [P, P])
        spare_i = sb("spare_i", [P, 1], I32)
        spare = sb("spare", [P, 1])
        ones_row = sb("ones_row", [1, P])
        pick_last = sb("pick_last", [1, D + 1])
        w_in = sb("w_in", [P, P])
        w_in_T = sb("w_in_T", [P, P])
        b_in = sb("b_in", [1, D])
        w1 = sb("w1", [P, D])
        b1_col = sb("b1_col", [D, 1])
        w2 = sb("w2", [D + 1, D])
        w2T = sb("w2T", [D, D + 1])
        wg = sb("wg", [D, D])
        bg_row = sb("bg_row", [1, D])
        w2g = sb("w2g", [D + 1, 2 * D])

        ps_key = ctx.enter_context(nc.psum_tensor("ps_key", [P, 1024], F32))
        ps_T = ctx.enter_context(nc.psum_tensor("ps_T", [P, 1024], F32))
        ps_a = ps_T
        ps_out = ctx.enter_context(nc.psum_tensor("ps_out", [P, 1024], F32))
        ps_sums = ctx.enter_context(nc.psum_tensor("ps_sums", [P, 512], F32))
        ps_sum = ps_sums[:, 0:BT * ROW].rearrange("p (t f) -> p t f", f=ROW)
        proj = ps_out[:, 0:BT * P].rearrange("p (t f) -> p t f", f=P)

        loaded_edges = sem("loaded_edges")
        loaded_weights = sem("loaded_weights")
        built = sem("built")
        cleared_w_in = sem("cleared_w_in")
        zeros_ready = sem("zeros_ready")
        constants = sem("constants")
        spare_ready = sem("spare_ready")
        weights_T = sem("weights_T")
        w_copied = sem("w_copied")
        w2g_done = sem("w2g_done")
        w2g_ready = sem("w2g_ready")
        cleared = [[sem(f"cleared{ly}{k}") for k in range(2)] for ly in range(2)]
        keys_ready = sem("keys_ready")
        key_spread = sem("key_spread")
        take_ready = sem("take_ready")
        gathered = [sem(f"gathered{u}") for u in range(2)]
        nodes_loaded = [sem(f"nodes_loaded{u}") for u in range(2)]
        summed_rows = sem("summed_rows")
        mean_ready = sem("mean_ready")
        centred = sem("centred")
        squared = sem("squared")
        sq_summed = sem("sq_summed")
        newton = sem("newton")
        normed = sem("normed")
        transposed = sem("transposed")
        hT_ready = sem("hT_ready")
        hidden = sem("hidden")
        aT_ready = sem("aT_ready")
        projected = sem("projected")
        self_added = sem("self_added")
        gate_ready = sem("gate_ready")
        msg_ready = sem("msg_ready")
        later_ready = sem("later_ready")
        spare_step = sem("spare_step")
        put_ready = sem("put_ready")
        combined = sem("combined")
        summed_ready = sem("summed_ready")
        scattered = [[sem(f"scattered{ly}{k}") for k in range(2)] for ly in range(2)]
        pool_passed = sem("pool_passed")
        chunk_loaded = [sem(f"chunk_loaded{s}") for s in range(2)]
        chunk_step = sem("chunk_step")
        chunk_ready = sem("chunk_ready")
        stored_x1 = sem("stored_x1")
        stored_out = sem("stored_out")

        block = ctx.enter_context(nc.Block())

        def node_cols(a, c0, n):
            return a[0:P * COLS, :].rearrange("(p c) f -> p c f", p=P)[:, bass.ds(c0, n), :]

        @block.sync
        def _(sp):
            for w, e in enumerate((src, dst)):
                sp.dma_start(edges[:, w, :], e[0:P * COLS].rearrange("(p c) -> p c", p=P)).then_inc(loaded_edges, 16)
                sp.dma_start(edges_tail[:, w, :], e[P * COLS:N].unsqueeze(1)).then_inc(loaded_edges, 16)

            def load_nodes(b):
                until(sp, centred, slot_free(b))
                if b.tiles == BT:
                    cols = node_cols(x, b.pair * 2 * BT + b.u * BT, BT)
                    sp.dma_start(rows[:, b.u, :, 1, :], cols).then_inc(nodes_loaded[b.u], 16)
                    sp.dma_start(xs[:, bass.ds(b.pair * 2 * BT + b.u * BT, BT), :], cols).then_inc(nodes_loaded[b.u], 16)
                else:
                    sp.dma_start(rows[0:TAIL, b.u, 0, 1, :], x[P * COLS:N, :]).then_inc(nodes_loaded[b.u], 16)
                    sp.dma_start(xs_tail[:, :], x[P * COLS:N, :]).then_inc(nodes_loaded[b.u], 16)
                if not isinstance(b.pair, int) and b.u == 1:
                    w = LATE_ROWS * ROW // LATE_DMAS
                    for k in range(2):
                        piece = tables[1][k].rearrange("(p c) f -> p (c f)", p=P)[:, bass.ds((b.pair - PEELED) * w, w)]
                        sp.dma_start(piece, zeros[:, 0:w]).then_inc(cleared[1][k], 16)

            every_batch(sp, 0, load_nodes)

            for layer in range(2):
                for k in range(2):
                    sp.wait_ge(scattered[layer][k], 16 * scatters(PAIRS, 1, k))

                def load_chunk(pair, s):
                    done = layer * (CHUNKS + 1) + 2 * pair + s
                    until(sp, chunk_ready, done if layer and isinstance(pair, int) and s == 0 else done - 1)
                    for k, chunk in enumerate((chunk_a, chunk_b)):
                        sp.dma_start(chunk[:, s, :, :], node_cols(tables[layer][k], pair * 2 * CHUNK + s * CHUNK, CHUNK))\
                          .then_inc(chunk_loaded[s], 16)

                every_chunk(sp, load_chunk)
                sp.wait_ge(chunk_ready, layer * (CHUNKS + 1) + CHUNKS - 1)
                for k, chunk in enumerate((chunk_a, chunk_b)):
                    sp.dma_start(chunk[0:TAIL, 0, 0, :], tables[layer][k][P * COLS:N, :]).then_inc(chunk_loaded[0], 16)
            sp.wait_ge(stored_out, 16 * (CHUNKS + 1))

        @block.gpsimd
        def _(pool):
            pool.memset(ident[:, :], 0.0).then_inc(built, 1)
            pool.memset(lower[:, :], 1.0).then_inc(built, 1)
            pool.wait_ge(built, 2)
            pool.affine_select(out=ident[:, :], in_=ident[:, :], compare_op=ALU.not_equal, fill=1.0,
                               base=0, pattern=[[-1, P]], channel_multiplier=1).then_inc(built, 1)
            pool.affine_select(out=lower[:, :], in_=lower[:, :], compare_op=ALU.is_ge, fill=0.0,
                               base=0, pattern=[[-1, P]], channel_multiplier=1).then_inc(built, 1)
            pool.iota(spare_i[:, :], pattern=[[0, 1]], base=N, channel_multiplier=1).then_inc(built, 1)
            last_node = pool.to_reg(N - 1)
            last_row = pool.to_reg(N + P - 1)

            def gather(b, t, w):
                pool.indirect_dma_start(
                    rows[0:b.parts, b.u, t, w, :], None, (x1 if b.layer else x)[:, :],
                    bass.IndirectOffsetOnAxis(ap=take[0:b.parts, b.u, w, t:t + 1], axis=0),
                    bounds_check=last_node, oob_is_err=True, compute_op=ALU.bypass).then_inc(gathered[b.u], 16)

            def scatter(b, t):
                k = (b.u * BT + t) % 2
                done = scattered[b.layer][k]
                if isinstance(b.pair, int) and 2 * BT * b.pair + BT * b.u + t < 2:
                    pool.wait_ge(cleared[b.layer][k], 16 * (LATE_DMAS if b.layer else ZERO_DMAS))
                else:
                    pool.wait_ge(done, 16 * scatters(b.pair, b.u * BT + t, k))
                pool.sem_inc(pool_passed, 1)
                pool.indirect_dma_start(
                    tables[b.layer][k][:, :],
                    bass.IndirectOffsetOnAxis(ap=put[0:b.parts, b.u, t:t + 1], axis=0),
                    summed[0:b.parts, b.u, t, :], None,
                    bounds_check=last_row, oob_is_err=True, compute_op=ALU.add).then_inc(done, 16)

            def scatter_ready(b):
                pool.wait_ge(put_ready, b.g + 1)
                pool.wait_ge(summed_ready, b.g + 1)
                pool.sem_inc(pool_passed, 1)

            def step(b):
                pool.wait_ge(take_ready, b.g + 1)
                until(pool, centred, slot_free(b))
                pool.sem_inc(pool_passed, 1)
                old = before(b, 2)
                for t in range(BT):
                    if t < b.tiles:
                        for w in range(1 + b.layer):
                            gather(b, t, w)
                    if old:
                        if t == 0:
                            scatter_ready(old)
                        scatter(old, t)

            for layer in range(2):
                if layer:
                    pool.wait_ge(stored_x1, 16 * (CHUNKS + 1))
                    pool.sem_inc(pool_passed, 1)
                every_batch(pool, layer, step)
                for b in (batch(layer, PAIRS - 1, 1), tail(layer)):
                    scatter_ready(b)
                    for t in range(b.tiles):
                        scatter(b, t)

        @block.vector
        def _(dve):
            nc.vector.memset(zeros[:, :], 0.0).then_inc(zeros_ready, 1)
            nc.vector.memset(w_in[:, :], 0.0).then_inc(cleared_w_in, 1)
            nc.vector.memset(ones_row[:, :], 1.0).then_inc(constants, 1)
            nc.vector.memset(pick_last[:, :], 0.0).then_inc(constants, 1)
            nc.vector.memset(aT[:, :], 1.0).then_inc(constants, 1)
            nc.vector.memset(msg[:, :, :], 1.0).then_inc(constants, 1)
            dve.wait_ge(constants, 2)
            nc.vector.memset(pick_last[:, D:D + 1], 1.0).then_inc(constants, 1)
            dve.wait_ge(built, 5)
            nc.vector.tensor_copy(spare[:, :], spare_i[:, :]).then_inc(spare_ready, 1)
            dve.wait_ge(loaded_edges, 64)

            def copy_indices(b):
                if b.tiles == BT:
                    nc.vector.tensor_copy(take[:, b.u, :, :], edges[:, :, bass.ds(b.pair * 2 * BT + b.u * BT, BT)])\
                      .then_inc(take_ready, 1)
                else:
                    nc.vector.tensor_copy(take[0:TAIL, b.u, :, 0:1], edges_tail[:, :, :]).then_inc(take_ready, 1)

            def finish(b):
                n, q = b.tiles, b.parts
                dve.wait_ge(later_ready, b.g + 1)
                nc.vector.tensor_scalar(to_spare[0:q, 0:n], key[0:q, b.u, 0:n], -1.0, spare[0:q, :],
                                        ALU.mult, ALU.add).then_inc(spare_step, 1)
                dve.wait_ge(spare_step, b.g * 2 + 1)
                nc.vector.scalar_tensor_tensor(out=shift[0:q, 0:n], in0=rank[0:q, b.u, 0:n], scalar=1.5,
                                               in1=to_spare[0:q, 0:n], op0=ALU.is_gt, op1=ALU.mult)\
                  .then_inc(spare_step, 1)
                dve.wait_ge(spare_step, b.g * 2 + 2)
                if not isinstance(b.pair, int) or b.pair > 0:
                    for k in range(2):
                        dve.wait_ge(scattered[b.layer][k], 16 * scatters(b.pair, b.u * BT - BT, k))
                nc.vector.tensor_tensor(put[0:q, b.u, 0:n], shift[0:q, 0:n], key[0:q, b.u, 0:n], ALU.add)\
                  .then_inc(put_ready, 1)
                dve.wait_ge(projected, b.g + 1)
                if b.layer == 0:
                    dve.wait_ge(msg_ready, b.g + 1)
                    mine = xs[:, bass.ds(b.pair * 2 * BT + b.u * BT, BT), :] if n == BT else xs_tail[:, :].unsqueeze(1)
                    nc.vector.tensor_tensor(mine, mine, proj[0:q, 0:n, D:2 * D], ALU.add).then_inc(self_added, 1)
                else:
                    dve.wait_ge(gate_ready, b.g - BATCHES + 1)
                    dve.wait_ge(combined, b.g)
                    nc.vector.tensor_tensor(msg[0:q, 0:n, 0:D], proj[0:q, 0:n, 0:D], gate[0:q, 0:n, :], ALU.mult)\
                      .then_inc(msg_ready, 1)

            def step(b):
                n, q, now = b.tiles, b.parts, b.g + 1
                way = b.layer == 0
                until(dve, key_spread, slot_free(b))
                until(dve, put_ready, slot_free(b))
                if n == BT:
                    own = edges[:, int(way), bass.ds(b.pair * 2 * BT + b.u * BT, BT)]
                else:
                    own = edges_tail[:, int(way), :]
                nc.vector.tensor_copy(key[0:q, b.u, 0:n], own).then_inc(keys_ready, 1)

                dve.wait_ge(gathered[b.u], gathered_by(b))
                if b.layer == 0:
                    dve.wait_ge(nodes_loaded[b.u], 32 * (b.pair + 1))
                raw = rows[0:q, b.u, 0:n, :, :].rearrange("p t w d -> p (t w) d")
                mid = xc[0:q, b.u, 0:n, :, :].rearrange("p t w d -> p (t w) d")
                r = slice(0, 2 * n)
                nc.vector.tensor_reduce(row_sum[0:q, r], raw, AX.X, ALU.add).then_inc(summed_rows, 1)
                dve.wait_ge(summed_rows, now)
                nc.vector.tensor_scalar(neg_mean[0:q, r], row_sum[0:q, r], -1.0 / D, None, ALU.mult)\
                  .then_inc(mean_ready, 1)
                until(dve, transposed, slot_free(b))
                dve.wait_ge(mean_ready, now)
                nc.vector.tensor_tensor(mid, raw, neg_mean[0:q, r].unsqueeze(2).to_broadcast([q, 2 * n, D]), ALU.add)\
                  .then_inc(centred, 1)
                following = after_next(b)
                if following:
                    copy_indices(following)

                until(dve, combined, slot_free(b))
                dve.wait_ge(key_spread, now)
                dve.wait_ge(keys_ready, now)
                for t in range(n):
                    last = nc.vector.scalar_tensor_tensor(
                        out=later[0:q, b.u, t, 0:q], in0=ps_key[0:q, t * P:t * P + q], scalar=key[0:q, b.u, t:t + 1],
                        in1=lower[0:q, 0:q], op0=ALU.is_equal, op1=ALU.mult, accum_out=rank[0:q, b.u, t:t + 1])
                last.then_inc(later_ready, 1)

                if before(b):
                    finish(before(b))

                dve.wait_ge(squared, now)
                nc.vector.tensor_reduce(sq_sum[0:q, r], sq[0:q, 0:n, :, :].rearrange("p t w d -> p (t w) d"), AX.X,
                                        ALU.add).then_inc(sq_summed, 1)
                dve.wait_ge(sq_summed, now)
                nc.vector.tensor_scalar(var[0:q, r], sq_sum[0:q, r], 1.0 / D, EPS, ALU.mult, ALU.add).then_inc(newton, 1)
                dve.wait_ge(newton, b.g * 12 + 1)
                nc.vector.tensor_scalar(half_bits[0:q, r], var[0:q, r].bitcast(I32), 1, None,
                                        ALU.logical_shift_right).then_inc(newton, 1)
                dve.wait_ge(newton, b.g * 12 + 2)
                nc.vector.tensor_scalar(guess[0:q, 0, r].bitcast(I32), half_bits[0:q, r], -1.0, float(0x5F3759DF),
                                        ALU.mult, ALU.add).then_inc(newton, 1)
                for k in range(3):
                    dve.wait_ge(newton, b.g * 12 + 3 + 3 * k)
                    nc.vector.tensor_tensor(y2[0:q, r], guess[0:q, k, r], guess[0:q, k, r], ALU.mult).then_inc(newton, 1)
                    dve.wait_ge(newton, b.g * 12 + 4 + 3 * k)
                    nc.vector.scalar_tensor_tensor(out=vy2[0:q, r], in0=y2[0:q, r], scalar=-0.5, in1=var[0:q, r],
                                                   op0=ALU.mult, op1=ALU.mult).then_inc(newton, 1)
                    dve.wait_ge(newton, b.g * 12 + 5 + 3 * k)
                    nc.vector.scalar_tensor_tensor(out=guess[0:q, k + 1, r], in0=vy2[0:q, r], scalar=1.5,
                                                   in1=guess[0:q, k, r], op0=ALU.add, op1=ALU.mult).then_inc(newton, 1)
                dve.wait_ge(newton, b.g * 12 + 12)
                nc.vector.tensor_tensor(mid, mid, guess[0:q, 3, r].unsqueeze(2).to_broadcast([q, 2 * n, D]), ALU.mult)\
                  .then_inc(normed, 1)

            for layer in range(2):
                for u in range(2):
                    copy_indices(batch(layer, 0, u))
                every_batch(dve, layer, step)
                finish(tail(layer))

                def merge_chunk(layer, a, b, mine, q, n, loads, s, at):
                    dve.wait_ge(chunk_loaded[s], loads)
                    nc.vector.tensor_tensor(count[0:q, 0:n], a[:, :, D], b[:, :, D], ALU.add).then_inc(chunk_step, 1)
                    nc.vector.tensor_tensor(a[:, :, 0:D], a[:, :, 0:D], b[:, :, 0:D], ALU.add).then_inc(chunk_step, 1)
                    dve.wait_ge(chunk_step, at * 5 + 1)
                    nc.vector.tensor_scalar(count1[0:q, 0:n], count[0:q, 0:n], 1.0, None, ALU.max).then_inc(chunk_step, 1)
                    dve.wait_ge(chunk_step, at * 5 + 3)
                    nc.vector.reciprocal(per_count[0:q, 0:n], count1[0:q, 0:n]).then_inc(chunk_step, 1)
                    dve.wait_ge(chunk_step, at * 5 + 4)
                    nc.vector.tensor_tensor(a[:, :, 0:D], a[:, :, 0:D],
                                            per_count[0:q, 0:n].unsqueeze(2).to_broadcast([q, n, D]), ALU.mult)\
                      .then_inc(chunk_step, 1)
                    dve.wait_ge(chunk_step, at * 5 + 5)
                    nc.vector.tensor_tensor(mine, mine, a[:, :, 0:D], ALU.add).then_inc(chunk_ready, 1)

                dve.wait_ge(self_added, BATCHES)

                def step_chunk(pair, s, layer=layer):
                    loads = 32 * (layer * (CHUNKS // 2 + (s == 0)) + pair + 1)
                    merge_chunk(layer, chunk_a[:, s, :, :], chunk_b[:, s, :, :],
                                xs[:, bass.ds(pair * 2 * CHUNK + s * CHUNK, CHUNK), :], P, CHUNK, loads, s,
                                layer * (CHUNKS + 1) + 2 * pair + s)

                every_chunk(dve, step_chunk)
                merge_chunk(layer, chunk_a[0:TAIL, 0, 0:1, :], chunk_b[0:TAIL, 0, 0:1, :], xs_tail[:, :].unsqueeze(1),
                            TAIL, 1, 32 * (layer + 1) * (CHUNKS // 2 + 1), 0, layer * (CHUNKS + 1) + CHUNKS)

        @block.scalar
        def _(act):
            act.wait_ge(zeros_ready, 1)
            for c in range(ZERO_DMAS):
                for k in range(2):
                    w = ZERO_ROWS * ROW // ZERO_DMAS
                    act.dma_start(tables[0][k].rearrange("(p c) f -> p (c f)", p=P)[:, c * w:(c + 1) * w],
                                  zeros[:, :]).then_inc(cleared[0][k], 16)
                if c == 0:
                    act.wait_ge(cleared_w_in, 1)
                    act.dma_start(w_in[0:D, 0:D], w_neigh[:, :]).then_inc(loaded_weights, 16)
                    act.dma_start(w_in[D:P, D:P], w_self[:, :]).then_inc(loaded_weights, 16)
                    act.dma_start(b_in[:, :], b_self.unsqueeze(0)).then_inc(loaded_weights, 16)
                    act.dma_start(w1[:, :], W1[:, :]).then_inc(loaded_weights, 16)
                    act.dma_start(b1_col[:, :], b1.unsqueeze(1)).then_inc(loaded_weights, 16)
                    act.dma_start(w2[0:D, :], W2[:, :]).then_inc(loaded_weights, 16)
                    act.dma_start(w2[D:D + 1, :], b2.unsqueeze(0)).then_inc(loaded_weights, 16)
                    act.dma_start(wg[:, :], Wg[:, :]).then_inc(loaded_weights, 16)
                    act.dma_start(bg_row[:, :], bg.unsqueeze(0)).then_inc(loaded_weights, 16)
            act.wait_ge(weights_T, 1)
            nc.scalar.activation(w_in_T[:, :], ps_T[:, 0:P], ACT.Copy).then_inc(w_copied, 1)
            nc.scalar.activation(w2T[:, :], ps_T[0:D, P:P + D + 1], ACT.Copy).then_inc(w_copied, 1)
            nc.scalar.activation(w2g[:, 0:D], w2[:, :], ACT.Copy).then_inc(w2g_ready, 1)
            act.wait_ge(w2g_done, 1)
            nc.scalar.activation(w2g[:, D:2 * D], ps_out[0:D + 1, 0:D], ACT.Copy).then_inc(w2g_ready, 1)

            def take_sums(b):
                act.wait_ge(combined, b.g + 1)
                if not isinstance(b.pair, int) or b.pair > 0:
                    for k in range(2):
                        act.wait_ge(scattered[b.layer][k], 16 * scatters(b.pair, b.u * BT - BT, k))
                nc.scalar.activation(summed[0:b.parts, b.u, 0:b.tiles, :], ps_sum[0:b.parts, 0:b.tiles, :], ACT.Copy)\
                  .then_inc(summed_ready, 1)

            def step(b):
                n, q, now = b.tiles, b.parts, b.g + 1
                until(act, sq_summed, b.g)
                act.wait_ge(centred, now)
                nc.scalar.activation(sq[0:q, 0:n, :, :], xc[0:q, b.u, 0:n, :, :], ACT.Square).then_inc(squared, 1)
                if before(b):
                    take_sums(before(b))
                until(act, projected, b.g)
                act.wait_ge(transposed, now)
                w = (n - 1) * P + q
                nc.scalar.activation(hT[:, 0:w], ps_T[:, 0:w], ACT.Relu).then_inc(hT_ready, 1)
                if b.layer == 0:
                    until(act, combined, b.g)
                    act.wait_ge(projected, now)
                    nc.scalar.activation(msg[0:q, 0:n, 0:D], proj[0:q, 0:n, 0:D], ACT.Copy).then_inc(msg_ready, 1)
                else:
                    act.wait_ge(hidden, b.g - BATCHES + 1)
                    nc.scalar.activation(aT[0:D, 0:w], ps_a[0:D, 0:w], ACT.Relu, bias=b1_col[:, :]).then_inc(aT_ready, 1)
                    act.wait_ge(msg_ready, b.g)
                    act.wait_ge(projected, now)
                    nc.scalar.activation(gate[0:q, 0:n, :], proj[0:q, 0:n, D:2 * D], ACT.Sigmoid).then_inc(gate_ready, 1)

            for layer, (result, stored) in enumerate(((x1, stored_x1), (out, stored_out))):
                every_batch(act, layer, step)
                take_sums(tail(layer))

                def store_chunk(pair, s):
                    act.wait_ge(chunk_ready, layer * (CHUNKS + 1) + 2 * pair + s + 1)
                    c = pair * 2 * CHUNK + s * CHUNK
                    act.dma_start(node_cols(result, c, CHUNK), xs[:, bass.ds(c, CHUNK), :]).then_inc(stored, 16)

                every_chunk(act, store_chunk)
                act.wait_ge(chunk_ready, (layer + 1) * (CHUNKS + 1))
                act.dma_start(result[P * COLS:N, :], xs_tail[:, :]).then_inc(stored, 16)
            act.wait_ge(stored_out, 16 * (CHUNKS + 1))

        @block.tensor
        def _(pe):
            pe.wait_ge(built, 5)
            pe.wait_ge(loaded_weights, 16 * 9)
            nc.tensor.transpose(ps_T[:, 0:P], w_in[:, :], ident[:, :])
            nc.tensor.transpose(ps_T[0:D, P:P + D + 1], w2[:, :], ident[0:D + 1, 0:D + 1]).then_inc(weights_T, 1)
            pe.wait_ge(constants, 5)
            pe.wait_ge(w_copied, 2)
            nc.tensor.matmul(ps_out[0:D + 1, 0:D], w2T[:, :], wg[:, :], start=True, stop=False)
            nc.tensor.matmul(ps_out[0:D + 1, 0:D], pick_last[:, :], bg_row[:, :], start=False, stop=True)\
              .then_inc(w2g_done, 1)
            pe.wait_ge(w2g_ready, 2)

            def combine(b):
                pe.wait_ge(later_ready, b.g + 1)
                pe.wait_ge(msg_ready, b.g + 1)
                until(pe, summed_ready, b.g)
                for t in range(b.tiles):
                    last = nc.tensor.matmul(ps_sum[0:b.parts, t, :], later[0:b.parts, b.u, t, 0:b.parts],
                                            msg[0:b.parts, t, :], start=True, stop=True)
                last.then_inc(combined, 1)

            def step(b):
                n, q, now = b.tiles, b.parts, b.g + 1
                until(pe, later_ready, b.g)
                pe.wait_ge(keys_ready, now)
                for t in range(n):
                    last = nc.tensor.transpose(ps_key[0:q, t * P:t * P + q], key[0:q, b.u, t:t + 1].to_broadcast([q, q]),
                                               ident[0:q, 0:q])
                last.then_inc(key_spread, 1)
                if before(b):
                    combine(before(b))
                until(pe, hT_ready, b.g)
                pe.wait_ge(normed, now)
                for t in range(n):
                    last = nc.tensor.transpose(ps_T[:, t * P:t * P + q],
                                               xc[0:q, b.u, t, :, :].rearrange("p w d -> p (w d)"), ident[0:q, 0:q])
                last.then_inc(transposed, 1)
                until(pe, msg_ready, b.g)
                if b.layer == 0:
                    until(pe, self_added, b.g)
                    pe.wait_ge(hT_ready, now)
                    for t in range(n):
                        nc.tensor.matmul(proj[0:q, t, :], hT[:, t * P:t * P + q], w_in_T[:, :], start=True, stop=False)
                        last = nc.tensor.matmul(proj[0:q, t, D:2 * D], ones_row[:, 0:q], b_in[:, :], start=False,
                                                stop=True)
                    last.then_inc(projected, 1)
                else:
                    until(pe, aT_ready, b.g - BATCHES)
                    pe.wait_ge(hT_ready, now)
                    w = (n - 1) * P + q
                    for lo in range(0, w, 512):
                        hi = min(w, lo + 512)
                        last = nc.tensor.matmul(ps_a[0:D, lo:hi], w1[:, :], hT[:, lo:hi], start=True, stop=True)
                    last.then_inc(hidden, 1)
                    pe.wait_ge(aT_ready, b.g - BATCHES + 1)
                    for t in range(n):
                        last = nc.tensor.matmul(proj[0:q, t, :], aT[:, t * P:t * P + q], w2g[:, :], start=True,
                                                stop=True)
                    last.then_inc(projected, 1)

            for layer in range(2):
                every_batch(pe, layer, step)
                combine(tail(layer))


_INS = ['x', 'src', 'dst', 'L0_gnn_w_neigh', 'L0_gnn_w_self', 'L0_gnn_b_self', 'L1_gnn_W1', 'L1_gnn_b1', 'L1_gnn_W2',
        'L1_gnn_b2', 'L1_gnn_Wg', 'L1_gnn_bg']


def kernel(**inputs):
    import concourse.bacc as _bacc
    from concourse.bass_utils import run_bass_kernel_spmd as _run

    nc = _bacc.Bacc("TRN2", target_bir_lowering=False, num_devices=1)
    arrays, args = {}, []
    for name in _INS:
        a = np.ascontiguousarray(inputs[name])
        arrays[f"in_{name}_dram"] = a
        args.append(nc.dram_tensor(f"in_{name}_dram", a.shape, mybir.dt.from_np(a.dtype), kind="ExternalInput").ap())
    args.append(nc.dram_tensor("out_0_dram", (N, D), F32, kind="ExternalOutput").ap())
    build(nc, *args)
    return _run(nc, [arrays], core_ids=[0]).results[0]["out_0_dram"]
```

```python
from collections import namedtuple
from contextlib import ExitStack

import numpy as np

import concourse.bass as bass
from concourse import mybir

F32 = mybir.dt.float32
I32 = mybir.dt.int32
ALU = mybir.AluOpType
ACT = mybir.ActivationFunctionType
AX = mybir.AxisListType

N = 50000
D = 64
P = 128
COLS = N // P
TAIL = N - P * COLS
BT = 5
RING = 3
TRIPS = COLS // (RING * BT)
BATCHES = RING * TRIPS + 1
ROW = D + 1
PEELED = 2
ZERO_ROWS = 392
ZERO_DMAS = 14
LATE_ROWS = 414
LATE_DMAS = TRIPS - 1 - PEELED
CHUNK = 26
CHUNKS = COLS // CHUNK
CHUNK_RING = 3
LEAD = 1
EPS = 1e-5

Batch = namedtuple("Batch", "layer trip u g parts tiles")


def batch(layer, trip, u):
    return Batch(layer, trip, u, layer * BATCHES + RING * trip + u, P, BT)


def tail(layer):
    return Batch(layer, TRIPS, 0, layer * BATCHES + RING * TRIPS, TAIL, 1)


def before(b, back=1):
    if isinstance(b.trip, int) and RING * b.trip + b.u < back:
        return None
    at = b.u - back
    return batch(b.layer, b.trip + at // RING, at % RING)


def after(b, ahead):
    at = b.u + ahead
    if isinstance(b.trip, int) and RING * b.trip + at >= RING * TRIPS:
        return tail(b.layer) if RING * b.trip + at == RING * TRIPS else None
    return batch(b.layer, b.trip + at // RING, at % RING)


def slot_free(b):
    return b.g if b.layer and isinstance(b.trip, int) and b.trip == 0 and b.u == 0 else b.g - RING + 1


def gathered_by(b):
    earlier = (TRIPS * BT + (b.u == 0)) * b.layer
    return 16 * (earlier + (1 + b.layer) * (b.trip * BT + b.tiles))


def scatters(trip, tiles, table):
    while tiles < 0:
        trip, tiles = trip - 1, tiles + RING * BT
    return trip * ((RING * BT + 1 - table) // 2) + (tiles + 1 - table) // 2


def until(engine, semaphore, value):
    if isinstance(value, int) and value <= 0:
        return
    engine.wait_ge(semaphore, value)


def every_batch(engine, layer, step):
    for trip in range(PEELED):
        for u in range(RING):
            step(batch(layer, trip, u))
    with engine.Fori(PEELED, TRIPS - 1) as trip:
        for u in range(RING):
            step(batch(layer, trip, u))
    for u in range(RING):
        step(batch(layer, TRIPS - 1, u))
    step(tail(layer))


def every_chunk(engine, step):
    for s in range(CHUNK_RING):
        step(0, s)
    with engine.Fori(1, CHUNKS // CHUNK_RING) as turn:
        for s in range(CHUNK_RING):
            step(turn, s)


def build(nc, x, src, dst, w_neigh, w_self, b_self, W1, b1, W2, b2, Wg, bg, out):
    ctx = ExitStack()
    with ctx:
        def sb(name, shape, dt=F32):
            return ctx.enter_context(nc.sbuf_tensor(name, shape, dt))

        def sem(name):
            return ctx.enter_context(nc.semaphore(name))

        def dram(name, shape):
            return nc.dram_tensor(name, shape, F32, kind="Internal").ap()

        tables = [[dram("sums_in_a", [ZERO_ROWS * P, ROW]), dram("sums_in_b", [ZERO_ROWS * P, ROW])],
                  [dram("sums_out_a", [LATE_ROWS * P, ROW]), dram("sums_out_b", [LATE_ROWS * P, ROW])]]
        x1 = dram("x1", [N, D])

        xs = sb("xs", [P, COLS, D])
        xs_tail = sb("xs_tail", [TAIL, D])
        edges = sb("edges", [P, 2, COLS], I32)
        edges_tail = sb("edges_tail", [TAIL, 2, 1], I32)
        take = sb("take", [P, RING, 2, BT], I32)
        rows = sb("rows", [P, RING, BT, 2, D])
        xc = sb("xc", [P, RING, BT, 2, D])
        sq = sb("sq", [P, BT, 2, D])
        row_sum = sb("row_sum", [P, 2 * BT])
        sq_sum = sb("sq_sum", [P, 2 * BT])
        var = sb("var", [P, 2 * BT])
        half_bits = sb("half_bits", [P, 2 * BT], I32)
        guess = sb("guess", [P, 4, 2 * BT])
        y2 = sb("y2", [P, 2 * BT])
        vy2 = sb("vy2", [P, 2 * BT])
        hT = sb("hT", [P, BT * P])
        aT = sb("aT", [D + 1, BT * P])
        gate = sb("gate", [P, BT, D])
        msg = sb("msg", [P, BT, ROW])
        key = sb("key", [P, RING, BT])
        later = sb("later", [P, RING, BT, P])
        rank = sb("rank", [P, RING, BT])
        to_spare = sb("to_spare", [P, BT])
        shift = sb("shift", [P, BT])
        put = sb("put", [P, RING, BT], I32)
        summed = sb("summed", [P, RING, BT, ROW])
        chunk_a = sb("chunk_a", [P, CHUNK_RING, CHUNK, ROW])
        chunk_b = sb("chunk_b", [P, CHUNK_RING, CHUNK, ROW])
        count = sb("count", [P, CHUNK])
        count1 = sb("count1", [P, CHUNK])
        per_count = sb("per_count", [P, CHUNK])
        zeros = sb("zeros", [P, ZERO_ROWS * ROW // ZERO_DMAS])
        ident = sb("ident", [P, P])
        lower = sb("lower", [P, P])
        spare_i = sb("spare_i", [P, 1], I32)
        spare = sb("spare", [P, 1])
        ones_row = sb("ones_row", [1, P])
        pick_last = sb("pick_last", [1, D + 1])
        w_in = sb("w_in", [P, P])
        w_in_T = sb("w_in_T", [P, P])
        b_in = sb("b_in", [1, D])
        w1 = sb("w1", [P, D])
        b1_col = sb("b1_col", [D, 1])
        w2 = sb("w2", [D + 1, D])
        w2T = sb("w2T", [D, D + 1])
        wg = sb("wg", [D, D])
        bg_row = sb("bg_row", [1, D])
        w2g = sb("w2g", [D + 1, 2 * D])

        ps_key = ctx.enter_context(nc.psum_tensor("ps_key", [P, 1024], F32))
        ps_T = ctx.enter_context(nc.psum_tensor("ps_T", [P, 1024], F32))
        ps_a = ps_T
        ps_out = ctx.enter_context(nc.psum_tensor("ps_out", [P, 1024], F32))
        ps_sums = ctx.enter_context(nc.psum_tensor("ps_sums", [P, 512], F32))
        ps_sum = ps_sums[:, 0:BT * ROW].rearrange("p (t f) -> p t f", f=ROW)
        proj = ps_out[:, 0:BT * P].rearrange("p (t f) -> p t f", f=P)

        loaded_edges = sem("loaded_edges")
        loaded_weights = sem("loaded_weights")
        built = sem("built")
        cleared_w_in = sem("cleared_w_in")
        zeros_ready = sem("zeros_ready")
        constants = sem("constants")
        spare_ready = sem("spare_ready")
        weights_T = sem("weights_T")
        w_copied = sem("w_copied")
        w2g_done = sem("w2g_done")
        w2g_ready = sem("w2g_ready")
        cleared = [[sem(f"cleared{ly}{k}") for k in range(2)] for ly in range(2)]
        keys_ready = sem("keys_ready")
        key_spread = sem("key_spread")
        take_ready = sem("take_ready")
        gathered = [sem(f"gathered{u}") for u in range(RING)]
        nodes_loaded = [sem(f"nodes_loaded{u}") for u in range(RING)]
        summed_rows = sem("summed_rows")
        centred = sem("centred")
        squared = sem("squared")
        sq_summed = sem("sq_summed")
        newton = sem("newton")
        normed = sem("normed")
        transposed = sem("transposed")
        hT_ready = sem("hT_ready")
        hidden = sem("hidden")
        aT_ready = sem("aT_ready")
        projected = sem("projected")
        self_added = sem("self_added")
        gate_ready = sem("gate_ready")
        msg_ready = sem("msg_ready")
        later_ready = sem("later_ready")
        spare_step = sem("spare_step")
        put_ready = sem("put_ready")
        combined = sem("combined")
        summed_ready = sem("summed_ready")
        scattered = [[sem(f"scattered{ly}{k}") for k in range(2)] for ly in range(2)]
        pool_passed = sem("pool_passed")
        chunk_loaded = [sem(f"chunk_loaded{s}") for s in range(CHUNK_RING)]
        chunk_step = sem("chunk_step")
        chunk_ready = sem("chunk_ready")
        stored_x1 = sem("stored_x1")
        stored_out = sem("stored_out")

        block = ctx.enter_context(nc.Block())

        def node_cols(a, c0, n):
            return a[0:P * COLS, :].rearrange("(p c) f -> p c f", p=P)[:, bass.ds(c0, n), :]

        @block.sync
        def _(sp):
            for w, e in enumerate((src, dst)):
                sp.dma_start(edges[:, w, :], e[0:P * COLS].rearrange("(p c) -> p c", p=P)).then_inc(loaded_edges, 16)
                sp.dma_start(edges_tail[:, w, :], e[P * COLS:N].unsqueeze(1)).then_inc(loaded_edges, 16)

            def load_nodes(b):
                until(sp, centred, slot_free(b))
                if b.tiles == BT:
                    cols = node_cols(x, (b.trip * RING + b.u) * BT, BT)
                    sp.dma_start(rows[:, b.u, :, 1, :], cols).then_inc(nodes_loaded[b.u], 16)
                    sp.dma_start(xs[:, bass.ds((b.trip * RING + b.u) * BT, BT), :], cols).then_inc(nodes_loaded[b.u], 16)
                else:
                    sp.dma_start(rows[0:TAIL, b.u, 0, 1, :], x[P * COLS:N, :]).then_inc(nodes_loaded[b.u], 16)
                    sp.dma_start(xs_tail[:, :], x[P * COLS:N, :]).then_inc(nodes_loaded[b.u], 16)
                if not isinstance(b.trip, int) and b.u == 1:
                    w = LATE_ROWS * ROW // LATE_DMAS
                    for k in range(2):
                        piece = tables[1][k].rearrange("(p c) f -> p (c f)", p=P)[:, bass.ds((b.trip - PEELED) * w, w)]
                        sp.dma_start(piece, zeros[:, 0:w]).then_inc(cleared[1][k], 16)

            every_batch(sp, 0, load_nodes)

            for layer in range(2):
                for k in range(2):
                    sp.wait_ge(scattered[layer][k], 16 * scatters(TRIPS, 1, k))

                def load_chunk(turn, s):
                    done = layer * (CHUNKS + 1) + CHUNK_RING * turn + s
                    first = layer and isinstance(turn, int) and s == 0
                    until(sp, chunk_ready, done if first else done - CHUNK_RING + 1)
                    for k, chunk in enumerate((chunk_a, chunk_b)):
                        sp.dma_start(chunk[:, s, :, :], node_cols(tables[layer][k], (turn * CHUNK_RING + s) * CHUNK, CHUNK))\
                          .then_inc(chunk_loaded[s], 16)

                every_chunk(sp, load_chunk)
                sp.wait_ge(chunk_ready, layer * (CHUNKS + 1) + CHUNKS - CHUNK_RING + 1)
                for k, chunk in enumerate((chunk_a, chunk_b)):
                    sp.dma_start(chunk[0:TAIL, 0, 0, :], tables[layer][k][P * COLS:N, :]).then_inc(chunk_loaded[0], 16)
            sp.wait_ge(stored_out, 16 * (CHUNKS + 1))

        @block.gpsimd
        def _(pool):
            pool.memset(ident[:, :], 0.0).then_inc(built, 1)
            pool.memset(lower[:, :], 1.0).then_inc(built, 1)
            pool.wait_ge(built, 2)
            pool.affine_select(out=ident[:, :], in_=ident[:, :], compare_op=ALU.not_equal, fill=1.0,
                               base=0, pattern=[[-1, P]], channel_multiplier=1).then_inc(built, 1)
            pool.affine_select(out=lower[:, :], in_=lower[:, :], compare_op=ALU.is_ge, fill=0.0,
                               base=0, pattern=[[-1, P]], channel_multiplier=1).then_inc(built, 1)
            pool.iota(spare_i[:, :], pattern=[[0, 1]], base=N, channel_multiplier=1).then_inc(built, 1)
            last_node = pool.to_reg(N - 1)
            last_row = pool.to_reg(N + P - 1)

            def gather(b, t, w):
                pool.indirect_dma_start(
                    rows[0:b.parts, b.u, t, w, :], None, (x1 if b.layer else x)[:, :],
                    bass.IndirectOffsetOnAxis(ap=take[0:b.parts, b.u, w, t:t + 1], axis=0),
                    bounds_check=last_node, oob_is_err=True, compute_op=ALU.bypass).then_inc(gathered[b.u], 16)

            def scatter(b, t):
                k = (b.u * BT + t) % 2
                done = scattered[b.layer][k]
                if isinstance(b.trip, int) and (RING * b.trip + b.u) * BT + t < 2:
                    pool.wait_ge(cleared[b.layer][k], 16 * (LATE_DMAS if b.layer else ZERO_DMAS))
                else:
                    pool.wait_ge(done, 16 * scatters(b.trip, b.u * BT + t, k))
                pool.sem_inc(pool_passed, 1)
                pool.indirect_dma_start(
                    tables[b.layer][k][:, :],
                    bass.IndirectOffsetOnAxis(ap=put[0:b.parts, b.u, t:t + 1], axis=0),
                    summed[0:b.parts, b.u, t, :], None,
                    bounds_check=last_row, oob_is_err=True, compute_op=ALU.add).then_inc(done, 16)

            def scatter_ready(b):
                pool.wait_ge(put_ready, b.g + 1)
                pool.wait_ge(summed_ready, b.g + 1)
                pool.sem_inc(pool_passed, 1)

            def step(b):
                pool.wait_ge(take_ready, b.g + 1)
                until(pool, centred, slot_free(b))
                pool.sem_inc(pool_passed, 1)
                old = before(b, RING)
                for t in range(BT + LEAD):
                    if t < b.tiles:
                        for w in range(1 + b.layer):
                            gather(b, t, w)
                    if old and t >= LEAD:
                        if t == LEAD:
                            scatter_ready(old)
                        scatter(old, t - LEAD)

            for layer in range(2):
                if layer:
                    pool.wait_ge(stored_x1, 16 * (CHUNKS + 1))
                    pool.sem_inc(pool_passed, 1)
                every_batch(pool, layer, step)
                for b in (batch(layer, TRIPS - 1, 1), batch(layer, TRIPS - 1, 2), tail(layer)):
                    scatter_ready(b)
                    for t in range(b.tiles):
                        scatter(b, t)

        @block.vector
        def _(dve):
            nc.vector.memset(zeros[:, :], 0.0).then_inc(zeros_ready, 1)
            nc.vector.memset(w_in[:, :], 0.0).then_inc(cleared_w_in, 1)
            nc.vector.memset(ones_row[:, :], 1.0).then_inc(constants, 1)
            nc.vector.memset(pick_last[:, :], 0.0).then_inc(constants, 1)
            nc.vector.memset(aT[:, :], 1.0).then_inc(constants, 1)
            nc.vector.memset(msg[:, :, :], 1.0).then_inc(constants, 1)
            dve.wait_ge(constants, 2)
            nc.vector.memset(pick_last[:, D:D + 1], 1.0).then_inc(constants, 1)
            dve.wait_ge(built, 5)
            nc.vector.tensor_copy(spare[:, :], spare_i[:, :]).then_inc(spare_ready, 1)
            dve.wait_ge(loaded_edges, 64)

            def copy_indices(b):
                if b.tiles == BT:
                    nc.vector.tensor_copy(take[:, b.u, :, :], edges[:, :, bass.ds((b.trip * RING + b.u) * BT, BT)])\
                      .then_inc(take_ready, 1)
                else:
                    nc.vector.tensor_copy(take[0:TAIL, b.u, :, 0:1], edges_tail[:, :, :]).then_inc(take_ready, 1)

            def add_own_term(b):
                dve.wait_ge(projected, b.g + 1)
                dve.wait_ge(msg_ready, b.g + 1)
                mine = xs[:, bass.ds((b.trip * RING + b.u) * BT, BT), :] if b.tiles == BT else xs_tail[:, :].unsqueeze(1)
                nc.vector.tensor_tensor(mine, mine, proj[0:b.parts, 0:b.tiles, D:2 * D], ALU.add).then_inc(self_added, 1)

            def finish(b):
                n, q = b.tiles, b.parts
                dve.wait_ge(later_ready, b.g + 1)
                nc.vector.tensor_scalar(to_spare[0:q, 0:n], key[0:q, b.u, 0:n], -1.0, spare[0:q, :],
                                        ALU.mult, ALU.add).then_inc(spare_step, 1)
                dve.wait_ge(spare_step, b.g * 2 + 1)
                nc.vector.scalar_tensor_tensor(out=shift[0:q, 0:n], in0=rank[0:q, b.u, 0:n], scalar=1.5,
                                               in1=to_spare[0:q, 0:n], op0=ALU.is_gt, op1=ALU.mult)\
                  .then_inc(spare_step, 1)
                dve.wait_ge(spare_step, b.g * 2 + 2)
                if not isinstance(b.trip, int) or b.trip > 0:
                    for k in range(2):
                        dve.wait_ge(scattered[b.layer][k], 16 * scatters(b.trip, (b.u + 1 - RING) * BT, k))
                nc.vector.tensor_tensor(put[0:q, b.u, 0:n], shift[0:q, 0:n], key[0:q, b.u, 0:n], ALU.add)\
                  .then_inc(put_ready, 1)
                if b.layer:
                    dve.wait_ge(projected, b.g + 1)
                    dve.wait_ge(gate_ready, b.g - BATCHES + 1)
                    dve.wait_ge(combined, b.g)
                    nc.vector.tensor_tensor(msg[0:q, 0:n, 0:D], proj[0:q, 0:n, 0:D], gate[0:q, 0:n, :], ALU.mult)\
                      .then_inc(msg_ready, 1)

            def copy_keys(b):
                n, q = b.tiles, b.parts
                way = 1 - b.layer
                until(dve, key_spread, slot_free(b))
                until(dve, put_ready, slot_free(b))
                own = edges[:, way, bass.ds((b.trip * RING + b.u) * BT, BT)] if n == BT else edges_tail[:, way, :]
                nc.vector.tensor_scalar(key[0:q, b.u, 0:n], own, 1.0, None, ALU.mult).then_inc(keys_ready, 1)

            def find_groups(b, t):
                if b is None or t >= b.tiles:
                    return
                q = b.parts
                if t == 0:
                    until(dve, combined, slot_free(b))
                    dve.wait_ge(key_spread, b.g + 1)
                    dve.wait_ge(keys_ready, b.g + 1)
                found = nc.vector.scalar_tensor_tensor(
                    out=later[0:q, b.u, t, 0:q], in0=ps_key[0:q, t * P:t * P + q], scalar=key[0:q, b.u, t:t + 1],
                    in1=lower[0:q, 0:q], op0=ALU.is_equal, op1=ALU.mult, accum_out=rank[0:q, b.u, t:t + 1])
                if t == b.tiles - 1:
                    found.then_inc(later_ready, 1)

            def step(b):
                n, q, now = b.tiles, b.parts, b.g + 1
                dve.wait_ge(gathered[b.u], gathered_by(b))
                if b.layer == 0:
                    dve.wait_ge(nodes_loaded[b.u], 32 * (b.trip + 1))
                raw = rows[0:q, b.u, 0:n, :, :].rearrange("p t w d -> p (t w) d")
                mid = xc[0:q, b.u, 0:n, :, :].rearrange("p t w d -> p (t w) d")
                r = slice(0, 2 * n)
                nc.vector.tensor_reduce(row_sum[0:q, r], raw, AX.X, ALU.add).then_inc(summed_rows, 1)
                until(dve, transposed, slot_free(b))
                dve.wait_ge(summed_rows, now)
                nc.vector.scalar_tensor_tensor(out=mid, in0=row_sum[0:q, r].unsqueeze(2).to_broadcast([q, 2 * n, D]),
                                               scalar=-1.0 / D, in1=raw, op0=ALU.mult, op1=ALU.add)\
                  .then_inc(centred, 1)
                if after(b, RING):
                    copy_indices(after(b, RING))

                if before(b):
                    finish(before(b))
                if after(b, 2):
                    copy_keys(after(b, 2))

                following = after(b, 1)
                dve.wait_ge(squared, now)
                nc.vector.tensor_reduce(sq_sum[0:q, r], sq[0:q, 0:n, :, :].rearrange("p t w d -> p (t w) d"), AX.X,
                                        ALU.add).then_inc(sq_summed, 1)
                find_groups(following, 0)
                dve.wait_ge(sq_summed, now)
                nc.vector.tensor_scalar(var[0:q, r], sq_sum[0:q, r], 1.0 / D, EPS, ALU.mult, ALU.add).then_inc(newton, 1)
                find_groups(following, 1)
                dve.wait_ge(newton, b.g * 12 + 1)
                nc.vector.tensor_scalar(half_bits[0:q, r], var[0:q, r].bitcast(I32), 1, None,
                                        ALU.logical_shift_right).then_inc(newton, 1)
                find_groups(following, 2)
                dve.wait_ge(newton, b.g * 12 + 2)
                nc.vector.tensor_scalar(guess[0:q, 0, r].bitcast(I32), half_bits[0:q, r], -1.0, float(0x5F3759DF),
                                        ALU.mult, ALU.add).then_inc(newton, 1)
                for k in range(3):
                    if k < 2:
                        find_groups(following, 3 + k)
                    dve.wait_ge(newton, b.g * 12 + 3 + 3 * k)
                    nc.vector.tensor_tensor(y2[0:q, r], guess[0:q, k, r], guess[0:q, k, r], ALU.mult).then_inc(newton, 1)
                    dve.wait_ge(newton, b.g * 12 + 4 + 3 * k)
                    nc.vector.scalar_tensor_tensor(out=vy2[0:q, r], in0=y2[0:q, r], scalar=-0.5, in1=var[0:q, r],
                                                   op0=ALU.mult, op1=ALU.mult).then_inc(newton, 1)
                    dve.wait_ge(newton, b.g * 12 + 5 + 3 * k)
                    nc.vector.scalar_tensor_tensor(out=guess[0:q, k + 1, r], in0=vy2[0:q, r], scalar=1.5,
                                                   in1=guess[0:q, k, r], op0=ALU.add, op1=ALU.mult).then_inc(newton, 1)
                dve.wait_ge(newton, b.g * 12 + 12)
                nc.vector.tensor_tensor(mid, mid, guess[0:q, 3, r].unsqueeze(2).to_broadcast([q, 2 * n, D]), ALU.mult)\
                  .then_inc(normed, 1)
                if before(b) and b.layer == 0:
                    add_own_term(before(b))

            for layer in range(2):
                for u in range(RING):
                    copy_indices(batch(layer, 0, u))
                for u in range(2):
                    copy_keys(batch(layer, 0, u))
                for t in range(BT):
                    find_groups(batch(layer, 0, 0), t)
                every_batch(dve, layer, step)
                finish(tail(layer))
                if layer == 0:
                    add_own_term(tail(0))

                def merge_chunk(layer, a, b, mine, q, n, loads, s, at):
                    dve.wait_ge(chunk_loaded[s], loads)
                    nc.vector.tensor_tensor(count[0:q, 0:n], a[:, :, D], b[:, :, D], ALU.add).then_inc(chunk_step, 1)
                    nc.vector.tensor_tensor(a[:, :, 0:D], a[:, :, 0:D], b[:, :, 0:D], ALU.add).then_inc(chunk_step, 1)
                    dve.wait_ge(chunk_step, at * 5 + 1)
                    nc.vector.tensor_scalar(count1[0:q, 0:n], count[0:q, 0:n], 1.0, None, ALU.max).then_inc(chunk_step, 1)
                    dve.wait_ge(chunk_step, at * 5 + 3)
                    nc.vector.reciprocal(per_count[0:q, 0:n], count1[0:q, 0:n]).then_inc(chunk_step, 1)
                    dve.wait_ge(chunk_step, at * 5 + 4)
                    nc.vector.tensor_tensor(a[:, :, 0:D], a[:, :, 0:D],
                                            per_count[0:q, 0:n].unsqueeze(2).to_broadcast([q, n, D]), ALU.mult)\
                      .then_inc(chunk_step, 1)
                    dve.wait_ge(chunk_step, at * 5 + 5)
                    nc.vector.tensor_tensor(mine, mine, a[:, :, 0:D], ALU.add).then_inc(chunk_ready, 1)

                dve.wait_ge(self_added, BATCHES)

                def step_chunk(turn, s, layer=layer):
                    loads = 32 * (layer * (CHUNKS // CHUNK_RING + (s == 0)) + turn + 1)
                    merge_chunk(layer, chunk_a[:, s, :, :], chunk_b[:, s, :, :],
                                xs[:, bass.ds((turn * CHUNK_RING + s) * CHUNK, CHUNK), :], P, CHUNK, loads, s,
                                layer * (CHUNKS + 1) + CHUNK_RING * turn + s)

                every_chunk(dve, step_chunk)
                merge_chunk(layer, chunk_a[0:TAIL, 0, 0:1, :], chunk_b[0:TAIL, 0, 0:1, :], xs_tail[:, :].unsqueeze(1),
                            TAIL, 1, 32 * (layer + 1) * (CHUNKS // CHUNK_RING + 1), 0, layer * (CHUNKS + 1) + CHUNKS)

        @block.scalar
        def _(act):
            act.wait_ge(zeros_ready, 1)
            for c in range(ZERO_DMAS):
                for k in range(2):
                    w = ZERO_ROWS * ROW // ZERO_DMAS
                    act.dma_start(tables[0][k].rearrange("(p c) f -> p (c f)", p=P)[:, c * w:(c + 1) * w],
                                  zeros[:, :]).then_inc(cleared[0][k], 16)
                if c == 0:
                    act.wait_ge(cleared_w_in, 1)
                    act.dma_start(w_in[0:D, 0:D], w_neigh[:, :]).then_inc(loaded_weights, 16)
                    act.dma_start(w_in[D:P, D:P], w_self[:, :]).then_inc(loaded_weights, 16)
                    act.dma_start(b_in[:, :], b_self.unsqueeze(0)).then_inc(loaded_weights, 16)
                    act.dma_start(w1[:, :], W1[:, :]).then_inc(loaded_weights, 16)
                    act.dma_start(b1_col[:, :], b1.unsqueeze(1)).then_inc(loaded_weights, 16)
                    act.dma_start(w2[0:D, :], W2[:, :]).then_inc(loaded_weights, 16)
                    act.dma_start(w2[D:D + 1, :], b2.unsqueeze(0)).then_inc(loaded_weights, 16)
                    act.dma_start(wg[:, :], Wg[:, :]).then_inc(loaded_weights, 16)
                    act.dma_start(bg_row[:, :], bg.unsqueeze(0)).then_inc(loaded_weights, 16)
            act.wait_ge(weights_T, 1)
            nc.scalar.activation(w_in_T[:, :], ps_T[:, 0:P], ACT.Copy).then_inc(w_copied, 1)
            nc.scalar.activation(w2T[:, :], ps_T[0:D, P:P + D + 1], ACT.Copy).then_inc(w_copied, 1)
            nc.scalar.activation(w2g[:, 0:D], w2[:, :], ACT.Copy).then_inc(w2g_ready, 1)
            act.wait_ge(w2g_done, 1)
            nc.scalar.activation(w2g[:, D:2 * D], ps_out[0:D + 1, 0:D], ACT.Copy).then_inc(w2g_ready, 1)

            def take_projections(b):
                n, q = b.tiles, b.parts
                if b.layer == 0:
                    until(act, combined, b.g)
                    act.wait_ge(projected, b.g + 1)
                    nc.scalar.activation(msg[0:q, 0:n, 0:D], proj[0:q, 0:n, 0:D], ACT.Copy).then_inc(msg_ready, 1)
                else:
                    act.wait_ge(msg_ready, b.g)
                    act.wait_ge(projected, b.g + 1)
                    nc.scalar.activation(gate[0:q, 0:n, :], proj[0:q, 0:n, D:2 * D], ACT.Sigmoid).then_inc(gate_ready, 1)

            def take_sums(b):
                act.wait_ge(combined, b.g + 1)
                if not isinstance(b.trip, int) or b.trip > 0:
                    for k in range(2):
                        act.wait_ge(scattered[b.layer][k], 16 * scatters(b.trip, (b.u + 1 - RING) * BT, k))
                nc.scalar.activation(summed[0:b.parts, b.u, 0:b.tiles, :], ps_sum[0:b.parts, 0:b.tiles, :], ACT.Copy)\
                  .then_inc(summed_ready, 1)

            def step(b):
                n, q, now = b.tiles, b.parts, b.g + 1
                until(act, sq_summed, b.g)
                act.wait_ge(centred, now)
                nc.scalar.activation(sq[0:q, 0:n, :, :], xc[0:q, b.u, 0:n, :, :], ACT.Square).then_inc(squared, 1)
                if before(b):
                    take_projections(before(b))
                    take_sums(before(b))
                until(act, projected, b.g)
                act.wait_ge(transposed, now)
                w = (n - 1) * P + q
                nc.scalar.activation(hT[:, 0:w], ps_T[:, 0:w], ACT.Relu).then_inc(hT_ready, 1)
                if b.layer:
                    act.wait_ge(hidden, b.g - BATCHES + 1)
                    nc.scalar.activation(aT[0:D, 0:w], ps_a[0:D, 0:w], ACT.Relu, bias=b1_col[:, :]).then_inc(aT_ready, 1)

            for layer, (result, stored) in enumerate(((x1, stored_x1), (out, stored_out))):
                every_batch(act, layer, step)
                take_projections(tail(layer))
                take_sums(tail(layer))

                def store_chunk(turn, s):
                    act.wait_ge(chunk_ready, layer * (CHUNKS + 1) + CHUNK_RING * turn + s + 1)
                    c = (turn * CHUNK_RING + s) * CHUNK
                    act.dma_start(node_cols(result, c, CHUNK), xs[:, bass.ds(c, CHUNK), :]).then_inc(stored, 16)

                every_chunk(act, store_chunk)
                act.wait_ge(chunk_ready, (layer + 1) * (CHUNKS + 1))
                act.dma_start(result[P * COLS:N, :], xs_tail[:, :]).then_inc(stored, 16)
            act.wait_ge(stored_out, 16 * (CHUNKS + 1))

        @block.tensor
        def _(pe):
            pe.wait_ge(built, 5)
            pe.wait_ge(loaded_weights, 16 * 9)
            nc.tensor.transpose(ps_T[:, 0:P], w_in[:, :], ident[:, :])
            nc.tensor.transpose(ps_T[0:D, P:P + D + 1], w2[:, :], ident[0:D + 1, 0:D + 1]).then_inc(weights_T, 1)
            pe.wait_ge(constants, 5)
            pe.wait_ge(w_copied, 2)
            nc.tensor.matmul(ps_out[0:D + 1, 0:D], w2T[:, :], wg[:, :], start=True, stop=False)
            nc.tensor.matmul(ps_out[0:D + 1, 0:D], pick_last[:, :], bg_row[:, :], start=False, stop=True)\
              .then_inc(w2g_done, 1)
            pe.wait_ge(w2g_ready, 2)

            def spread_keys(b):
                until(pe, later_ready, b.g)
                pe.wait_ge(keys_ready, b.g + 1)
                for t in range(b.tiles):
                    last = nc.tensor.transpose(ps_key[0:b.parts, t * P:t * P + b.parts],
                                               key[0:b.parts, b.u, t:t + 1].to_broadcast([b.parts, b.parts]),
                                               ident[0:b.parts, 0:b.parts])
                last.then_inc(key_spread, 1)

            def combine(b):
                pe.wait_ge(later_ready, b.g + 1)
                pe.wait_ge(msg_ready, b.g + 1)
                until(pe, summed_ready, b.g)
                for t in range(b.tiles):
                    last = nc.tensor.matmul(ps_sum[0:b.parts, t, :], later[0:b.parts, b.u, t, 0:b.parts],
                                            msg[0:b.parts, t, :], start=True, stop=True)
                last.then_inc(combined, 1)

            def step(b):
                n, q, now = b.tiles, b.parts, b.g + 1
                if before(b):
                    combine(before(b))
                until(pe, hT_ready, b.g)
                pe.wait_ge(normed, now)
                for t in range(n):
                    last = nc.tensor.transpose(ps_T[:, t * P:t * P + q],
                                               xc[0:q, b.u, t, :, :].rearrange("p w d -> p (w d)"), ident[0:q, 0:q])
                last.then_inc(transposed, 1)
                if after(b, 2):
                    spread_keys(after(b, 2))
                until(pe, msg_ready, b.g)
                if b.layer == 0:
                    until(pe, self_added, b.g)
                    pe.wait_ge(hT_ready, now)
                    for t in range(n):
                        nc.tensor.matmul(proj[0:q, t, :], hT[:, t * P:t * P + q], w_in_T[:, :], start=True, stop=False)
                        last = nc.tensor.matmul(proj[0:q, t, D:2 * D], ones_row[:, 0:q], b_in[:, :], start=False,
                                                stop=True)
                    last.then_inc(projected, 1)
                else:
                    pe.wait_ge(hT_ready, now)
                    w = (n - 1) * P + q
                    for lo in range(0, w, 512):
                        hi = min(w, lo + 512)
                        last = nc.tensor.matmul(ps_a[0:D, lo:hi], w1[:, :], hT[:, lo:hi], start=True, stop=True)
                    last.then_inc(hidden, 1)
                    pe.wait_ge(aT_ready, b.g - BATCHES + 1)
                    for t in range(n):
                        last = nc.tensor.matmul(proj[0:q, t, :], aT[:, t * P:t * P + q], w2g[:, :], start=True,
                                                stop=True)
                    last.then_inc(projected, 1)

            for layer in range(2):
                for u in range(2):
                    spread_keys(batch(layer, 0, u))
                every_batch(pe, layer, step)
                combine(tail(layer))


_INS = ['x', 'src', 'dst', 'L0_gnn_w_neigh', 'L0_gnn_w_self', 'L0_gnn_b_self', 'L1_gnn_W1', 'L1_gnn_b1', 'L1_gnn_W2',
        'L1_gnn_b2', 'L1_gnn_Wg', 'L1_gnn_bg']


def kernel(**inputs):
    import concourse.bacc as _bacc
    from concourse.bass_utils import run_bass_kernel_spmd as _run

    nc = _bacc.Bacc("TRN2", target_bir_lowering=False, num_devices=1)
    arrays, args = {}, []
    for name in _INS:
        a = np.ascontiguousarray(inputs[name])
        arrays[f"in_{name}_dram"] = a
        args.append(nc.dram_tensor(f"in_{name}_dram", a.shape, mybir.dt.from_np(a.dtype), kind="ExternalInput").ap())
    args.append(nc.dram_tensor("out_0_dram", (N, D), F32, kind="ExternalOutput").ap())
    build(nc, *args)
    return _run(nc, [arrays], core_ids=[0]).results[0]["out_0_dram"]
```
